# Optimizing a Trainium2 kernel written in Bass

```python
import numpy as np
import jax
import jax.numpy as jnp

def _softmax(x, axis=-1):
    return jax.nn.softmax(x, axis=axis)

def _gelu(x):
    return jax.nn.gelu(x, approximate=True)

def _silu(x):
    return jax.nn.silu(x)

def _sigmoid(x):
    return jax.nn.sigmoid(x)

def _layernorm(x, axis=-1, eps=1e-05):
    m = jnp.mean(x, axis=axis, keepdims=True)
    v = jnp.var(x, axis=axis, keepdims=True)
    return (x - m) / jnp.sqrt(v + eps)

def _scatter_add(tgt, idx, src, axis=0):
    return tgt.at[idx].add(src)

def _segment_sum(src, seg, n):
    return jax.ops.segment_sum(src, seg, n)
kernel_name = 'mk_recurrent_d2_jaxref_r8_923da4'

def setup_inputs(seed: int=0):
    np.random.seed(seed)
    _w = jnp.asarray

    def _L0_attn_setup():
        import jax, jax.numpy as jnp
        import numpy as np
        EPS = 1e-06

        def _causal_depthwise_conv(x, conv_w, conv_b):
            B, L, d = x.shape
            lhs = jnp.transpose(x, (0, 2, 1))
            out = jax.lax.conv_general_dilated(lhs, conv_w, window_strides=(1,), padding=[(3, 0)], feature_group_count=d, dimension_numbers=('NCH', 'OIH', 'NCH'))
            out = out + conv_b[None, :, None]
            return jnp.transpose(out, (0, 2, 1))
        key = jax.random.key(seed)
        ks = jax.random.split(key, 8)
        B, L, d = (4, 512, 128)
        x = jax.random.normal(ks[0], (B, L, d), dtype=jnp.float32)
        conv_w = jax.random.normal(ks[1], (d, 1, 4), dtype=jnp.float32) * 0.02
        conv_b = jnp.zeros((d,), dtype=jnp.float32)
        lim = 1.0 / np.sqrt(d)
        W_r = jax.random.uniform(ks[2], (d, d), jnp.float32, -lim, lim)
        b_r = jax.random.uniform(ks[3], (d,), jnp.float32, -lim, lim)
        W_i = jax.random.uniform(ks[4], (d, d), jnp.float32, -lim, lim)
        b_i = jax.random.uniform(ks[5], (d,), jnp.float32, -lim, lim)
        log_a = jnp.full((d,), 7.5, dtype=jnp.float32)
        W_out = jax.random.uniform(ks[6], (d, d), jnp.float32, -lim, lim)
        gamma = jnp.ones((d,), dtype=jnp.float32)
        return {'x': x, 'conv_w': conv_w, 'conv_b': conv_b, 'W_r': W_r, 'b_r': b_r, 'W_i': W_i, 'b_i': b_i, 'log_a': log_a, 'W_out': W_out, 'gamma': gamma}
    _L0_attn_in = _L0_attn_setup()

    def _L0_ffn_setup():
        import jax, jax.numpy as jnp
        import numpy as np
        D = 128
        H = 16
        DK = D // H
        E = 8
        DFF = 4 * D
        TOPK = 2
        EPS = 1e-05

        def _layernorm(x, g, b):
            m = jnp.mean(x, axis=-1, keepdims=True)
            v = jnp.mean(jnp.square(x - m), axis=-1, keepdims=True)
            return (x - m) * jax.lax.rsqrt(v + EPS) * g + b
        key = jax.random.key(seed)
        ks = jax.random.split(key, 16)
        s_in = 1.0 / np.sqrt(D)
        s_ff = 1.0 / np.sqrt(DFF)
        return {'x': jax.random.normal(ks[0], (2, 256, D), dtype=jnp.float32), 'ln1_g': jnp.ones((D,), jnp.float32), 'ln1_b': jnp.zeros((D,), jnp.float32), 'w_qkv': jax.random.normal(ks[1], (D, 3 * D), jnp.float32) * s_in, 'b_qkv': jnp.zeros((3 * D,), jnp.float32), 'w_o': jax.random.normal(ks[2], (D, D), jnp.float32) * s_in, 'b_o': jnp.zeros((D,), jnp.float32), 'ln2_g': jnp.ones((D,), jnp.float32), 'ln2_b': jnp.zeros((D,), jnp.float32), 'gate_w': jax.random.normal(ks[3], (D, E), jnp.float32) * s_in, 'gate_b': jnp.zeros((E,), jnp.float32), 'W1': jax.random.normal(ks[4], (E, D, DFF), jnp.float32) * s_in, 'b1': jnp.zeros((E, DFF), jnp.float32), 'W2': jax.random.normal(ks[5], (E, DFF, D), jnp.float32) * s_ff, 'b2': jnp.zeros((E, D), jnp.float32)}
    _L0_ffn_in = _L0_ffn_setup()

    def _L1_attn_setup():
        import jax, jax.numpy as jnp
        import numpy as np
        DIM = 128
        H = 16
        D = DIM // H
        SCALE = D ** (-0.5)
        EPS = 1e-05

        def _layernorm(x, w, b):
            xf = x.astype(jnp.float32)
            mu = xf.mean(-1, keepdims=True)
            var = xf.var(-1, keepdims=True)
            y = (xf - mu) / jnp.sqrt(var + EPS) * w.astype(jnp.float32) + b.astype(jnp.float32)
            return y.astype(x.dtype)
        key = jax.random.key(seed)
        ks = jax.random.split(key, 8)
        x = jax.random.normal(ks[0], (2, 256, DIM), dtype=jnp.float32)
        qkv_w = jax.random.normal(ks[1], (3 * DIM, DIM), dtype=jnp.float32) * DIM ** (-0.5)
        q_norm_w = jnp.ones((D,), jnp.float32)
        q_norm_b = jnp.zeros((D,), jnp.float32)
        k_norm_w = jnp.ones((D,), jnp.float32)
        k_norm_b = jnp.zeros((D,), jnp.float32)
        proj_w = jax.random.normal(ks[2], (DIM, DIM), dtype=jnp.float32) * DIM ** (-0.5)
        proj_b = jnp.zeros((DIM,), jnp.float32)
        return {'x': x, 'qkv_w': qkv_w, 'q_norm_w': q_norm_w, 'q_norm_b': q_norm_b, 'k_norm_w': k_norm_w, 'k_norm_b': k_norm_b, 'proj_w': proj_w, 'proj_b': proj_b}
    _L1_attn_in = _L1_attn_setup()

    def _L1_ffn_setup():
        import jax, jax.numpy as jnp
        import numpy as np
        BLOCK = 16
        _GRID = jnp.array([0.0, 0.5, 1.0, 1.5, 2.0, 3.0, 4.0, 6.0], dtype=jnp.float32)
        _MID = jnp.array([0.25, 0.75, 1.25, 1.75, 2.5, 3.5, 5.0], dtype=jnp.float32)

        def fp4_quant_dequant(x):
            shape = x.shape
            xb = x.reshape(shape[:-1] + (shape[-1] // BLOCK, BLOCK))
            scale = jnp.max(jnp.abs(xb), axis=-1, keepdims=True) / 6.0
            scale = jnp.maximum(scale, jnp.float32(1e-12))
            xn = xb / scale
            idx = jnp.searchsorted(_MID, jnp.abs(xn))
            q = _GRID[idx] * jnp.sign(xn) * scale
            return q.reshape(shape)

        def fp4_linear(x, w):
            xq = fp4_quant_dequant(x)
            wq = fp4_quant_dequant(w)
            return jnp.einsum('bsk,nk->bsn', xq, wq)
        key = jax.random.key(seed)
        k1, k2, k3, k4 = jax.random.split(key, 4)
        H, I = (128, 352)
        x = jax.random.normal(k1, (4, 512, H), dtype=jnp.float32)
        w_gate = jax.random.normal(k2, (I, H), dtype=jnp.float32) * 0.02
        w_up = jax.random.normal(k3, (I, H), dtype=jnp.float32) * 0.02
        w_down = jax.random.normal(k4, (H, I), dtype=jnp.float32) * 0.02
        return {'x': x, 'w_gate': w_gate, 'w_up': w_up, 'w_down': w_down}
    _L1_ffn_in = _L1_ffn_setup()
    _d = {'L0_attn_x': _L0_attn_in['x'], 'L0_attn_conv_w': _L0_attn_in['conv_w'], 'L0_attn_conv_b': _L0_attn_in['conv_b'], 'L0_attn_W_r': _L0_attn_in['W_r'], 'L0_attn_b_r': _L0_attn_in['b_r'], 'L0_attn_W_i': _L0_attn_in['W_i'], 'L0_attn_b_i': _L0_attn_in['b_i'], 'L0_attn_log_a': _L0_attn_in['log_a'], 'L0_attn_W_out': _L0_attn_in['W_out'], 'L0_attn_gamma': _L0_attn_in['gamma'], 'L0_ffn_ln1_g': _L0_ffn_in['ln1_g'], 'L0_ffn_ln1_b': _L0_ffn_in['ln1_b'], 'L0_ffn_w_qkv': _L0_ffn_in['w_qkv'], 'L0_ffn_b_qkv': _L0_ffn_in['b_qkv'], 'L0_ffn_w_o': _L0_ffn_in['w_o'], 'L0_ffn_b_o': _L0_ffn_in['b_o'], 'L0_ffn_ln2_g': _L0_ffn_in['ln2_g'], 'L0_ffn_ln2_b': _L0_ffn_in['ln2_b'], 'L0_ffn_gate_w': _L0_ffn_in['gate_w'], 'L0_ffn_gate_b': _L0_ffn_in['gate_b'], 'L0_ffn_W1': _L0_ffn_in['W1'], 'L0_ffn_b1': _L0_ffn_in['b1'], 'L0_ffn_W2': _L0_ffn_in['W2'], 'L0_ffn_b2': _L0_ffn_in['b2'], 'L1_attn_qkv_w': _L1_attn_in['qkv_w'], 'L1_attn_q_norm_w': _L1_attn_in['q_norm_w'], 'L1_attn_q_norm_b': _L1_attn_in['q_norm_b'], 'L1_attn_k_norm_w': _L1_attn_in['k_norm_w'], 'L1_attn_k_norm_b': _L1_attn_in['k_norm_b'], 'L1_attn_proj_w': _L1_attn_in['proj_w'], 'L1_attn_proj_b': _L1_attn_in['proj_b'], 'L1_ffn_w_gate': _L1_ffn_in['w_gate'], 'L1_ffn_w_up': _L1_ffn_in['w_up'], 'L1_ffn_w_down': _L1_ffn_in['w_down']}
    _x0 = _d['L0_attn_x']
    _d['L0_attn_x'] = jax.random.normal(jax.random.fold_in(jax.random.key(seed), 1), (16, 256, 128), dtype=_x0.dtype)
    del _x0
    return _d

def reference(L0_attn_x, L0_attn_conv_w, L0_attn_conv_b, L0_attn_W_r, L0_attn_b_r, L0_attn_W_i, L0_attn_b_i, L0_attn_log_a, L0_attn_W_out, L0_attn_gamma, L0_ffn_ln1_g, L0_ffn_ln1_b, L0_ffn_w_qkv, L0_ffn_b_qkv, L0_ffn_w_o, L0_ffn_b_o, L0_ffn_ln2_g, L0_ffn_ln2_b, L0_ffn_gate_w, L0_ffn_gate_b, L0_ffn_W1, L0_ffn_b1, L0_ffn_W2, L0_ffn_b2, L1_attn_qkv_w, L1_attn_q_norm_w, L1_attn_q_norm_b, L1_attn_k_norm_w, L1_attn_k_norm_b, L1_attn_proj_w, L1_attn_proj_b, L1_ffn_w_gate, L1_ffn_w_up, L1_ffn_w_down):

    def _L0_attn_ref(x, conv_w, conv_b, W_r, b_r, W_i, b_i, log_a, W_out, gamma):
        import jax, jax.numpy as jnp
        import numpy as np
        EPS = 1e-06

        def _causal_depthwise_conv(x, conv_w, conv_b):
            B, L, d = x.shape
            lhs = jnp.transpose(x, (0, 2, 1))
            out = jax.lax.conv_general_dilated(lhs, conv_w, window_strides=(1,), padding=[(3, 0)], feature_group_count=d, dimension_numbers=('NCH', 'OIH', 'NCH'))
            out = out + conv_b[None, :, None]
            return jnp.transpose(out, (0, 2, 1))
        B, L, d = x.shape
        x_conv = _causal_depthwise_conv(x, conv_w, conv_b)
        r_t = jax.nn.sigmoid(x_conv @ W_r.T + b_r)
        i_t = jax.nn.sigmoid(x_conv @ W_i.T + b_i)
        a_base = jax.nn.sigmoid(log_a)
        a_t = a_base[None, None, :] ** (8.0 * r_t)
        inp = i_t * x_conv
        scale = jnp.sqrt(jnp.clip(1.0 - a_t * a_t, 0.0))

        def step(h, ab):
            a, b = ab
            h = a * h + b
            return (h, h)
        xs = (jnp.moveaxis(a_t, 1, 0), jnp.moveaxis(scale * inp, 1, 0))
        h0 = jnp.zeros((B, d), dtype=x.dtype)
        _, hs = jax.lax.scan(step, h0, xs)
        out = jnp.moveaxis(hs, 0, 1)
        out = out @ W_out.T
        rms = jax.lax.rsqrt(jnp.mean(out * out, axis=-1, keepdims=True) + EPS)
        return out * rms * gamma

    def _L0_ffn_ref(x, ln1_g, ln1_b, w_qkv, b_qkv, w_o, b_o, ln2_g, ln2_b, gate_w, gate_b, W1, b1, W2, b2):
        import jax, jax.numpy as jnp
        import numpy as np
        D = 128
        H = 16
        DK = D // H
        E = 8
        DFF = 4 * D
        TOPK = 2
        EPS = 1e-05

        def _layernorm(x, g, b):
            m = jnp.mean(x, axis=-1, keepdims=True)
            v = jnp.mean(jnp.square(x - m), axis=-1, keepdims=True)
            return (x - m) * jax.lax.rsqrt(v + EPS) * g + b
        B, S, _ = x.shape
        h = _layernorm(x, ln1_g, ln1_b)
        qkv = h @ w_qkv + b_qkv
        q, k, v = jnp.split(qkv, 3, axis=-1)
        q = q.reshape(B, S, H, DK)
        k = k.reshape(B, S, H, DK)
        v = v.reshape(B, S, H, DK)
        scores = jnp.einsum('bqhd,bkhd->bhqk', q, k) / np.sqrt(DK)
        attn = jax.nn.softmax(scores, axis=-1)
        o = jnp.einsum('bhqk,bkhd->bqhd', attn, v).reshape(B, S, D)
        x = x + o @ w_o + b_o
        h = _layernorm(x, ln2_g, ln2_b).reshape(B * S, D)
        logits = h @ gate_w + gate_b
        topv, topi = jax.lax.top_k(logits, TOPK)
        gw = jax.nn.softmax(topv, axis=-1)
        ew = jnp.sum(jax.nn.one_hot(topi, E, dtype=h.dtype) * gw[..., None], axis=1)
        hid = jax.nn.relu(jnp.einsum('td,edf->etf', h, W1) + b1[:, None, :])
        out_e = jnp.einsum('etf,efd->etd', hid, W2) + b2[:, None, :]
        moe = jnp.einsum('etd,te->td', out_e, ew)
        return x + moe.reshape(B, S, D)

    def _L1_attn_ref(x, qkv_w, q_norm_w, q_norm_b, k_norm_w, k_norm_b, proj_w, proj_b):
        import jax, jax.numpy as jnp
        import numpy as np
        DIM = 128
        H = 16
        D = DIM // H
        SCALE = D ** (-0.5)
        EPS = 1e-05

        def _layernorm(x, w, b):
            xf = x.astype(jnp.float32)
            mu = xf.mean(-1, keepdims=True)
            var = xf.var(-1, keepdims=True)
            y = (xf - mu) / jnp.sqrt(var + EPS) * w.astype(jnp.float32) + b.astype(jnp.float32)
            return y.astype(x.dtype)
        B, N, C = x.shape
        qkv = x @ qkv_w.T
        qkv = qkv.reshape(B, N, 3, H, D).transpose(2, 0, 3, 1, 4)
        q, k, v = (qkv[0], qkv[1], qkv[2])
        q = _layernorm(q, q_norm_w, q_norm_b)
        k = _layernorm(k, k_norm_w, k_norm_b)
        k = k - k.mean(-2, keepdims=True)
        attn = jnp.einsum('bhnd,bhmd->bhnm', q * SCALE, k)
        attn = attn - attn.max(-1, keepdims=True)
        attn = jax.nn.softmax(attn, axis=-1)
        out = jnp.einsum('bhnm,bhmd->bhnd', attn, v)
        out = out.transpose(0, 2, 1, 3).reshape(B, N, C)
        return out @ proj_w.T + proj_b

    def _L1_ffn_ref(x, w_gate, w_up, w_down):
        import jax, jax.numpy as jnp
        import numpy as np
        BLOCK = 16
        _GRID = jnp.array([0.0, 0.5, 1.0, 1.5, 2.0, 3.0, 4.0, 6.0], dtype=jnp.float32)
        _MID = jnp.array([0.25, 0.75, 1.25, 1.75, 2.5, 3.5, 5.0], dtype=jnp.float32)

        def fp4_quant_dequant(x):
            shape = x.shape
            xb = x.reshape(shape[:-1] + (shape[-1] // BLOCK, BLOCK))
            scale = jnp.max(jnp.abs(xb), axis=-1, keepdims=True) / 6.0
            scale = jnp.maximum(scale, jnp.float32(1e-12))
            xn = xb / scale
            idx = jnp.searchsorted(_MID, jnp.abs(xn))
            q = _GRID[idx] * jnp.sign(xn) * scale
            return q.reshape(shape)

        def fp4_linear(x, w):
            xq = fp4_quant_dequant(x)
            wq = fp4_quant_dequant(w)
            return jnp.einsum('bsk,nk->bsn', xq, wq)
        gate = fp4_linear(x, w_gate)
        y = fp4_linear(x, w_up)
        h = jax.nn.silu(gate) * y
        return fp4_linear(h, w_down)
    x = L0_attn_x
    xn = _layernorm(x, axis=-1)
    s = _L0_attn_ref(xn, L0_attn_conv_w, L0_attn_conv_b, L0_attn_W_r, L0_attn_b_r, L0_attn_W_i, L0_attn_b_i, L0_attn_log_a, L0_attn_W_out, L0_attn_gamma)
    g = _silu(_L0_ffn_ref(xn, L0_ffn_ln1_g, L0_ffn_ln1_b, L0_ffn_w_qkv, L0_ffn_b_qkv, L0_ffn_w_o, L0_ffn_b_o, L0_ffn_ln2_g, L0_ffn_ln2_b, L0_ffn_gate_w, L0_ffn_gate_b, L0_ffn_W1, L0_ffn_b1, L0_ffn_W2, L0_ffn_b2))
    x = x + s * g
    xn = _layernorm(x, axis=-1)
    s = _L1_attn_ref(xn, L1_attn_qkv_w, L1_attn_q_norm_w, L1_attn_q_norm_b, L1_attn_k_norm_w, L1_attn_k_norm_b, L1_attn_proj_w, L1_attn_proj_b)
    g = _silu(_L1_ffn_ref(xn, L1_ffn_w_gate, L1_ffn_w_up, L1_ffn_w_down))
    x = x + s * g
    return x

_drawn_inputs = setup_inputs


def setup_inputs(seed=0):
    import zlib

    import numpy as np

    out = dict(_drawn_inputs(seed))
    spreads = {'L0_attn_conv_b': (0.0, 0.1),
     'L0_attn_log_a': (7.5, 0.2),
     'L0_attn_gamma': (1.0, 0.2),
     'L0_ffn_ln1_g': (1.0, 0.2),
     'L0_ffn_ln1_b': (0.0, 0.1),
     'L0_ffn_b_qkv': (0.0, 0.1),
     'L0_ffn_b_o': (0.0, 0.1),
     'L0_ffn_ln2_g': (1.0, 0.2),
     'L0_ffn_ln2_b': (0.0, 0.1),
     'L0_ffn_gate_b': (0.0, 0.1),
     'L0_ffn_b1': (0.0, 0.297),
     'L0_ffn_b2': (0.0, 0.1),
     'L1_attn_q_norm_w': (1.0, 0.6),
     'L1_attn_q_norm_b': (0.0, 0.8),
     'L1_attn_k_norm_w': (1.0, 0.6),
     'L1_attn_k_norm_b': (0.0, 0.8),
     'L1_attn_proj_b': (0.0, 0.8)}
    factors = {'L0_attn_W_r': 7.998,
     'L0_attn_b_r': 8.0,
     'L0_attn_W_i': 3.138,
     'L0_attn_b_i': 3.179,
     'L1_attn_qkv_w': 8.0,
     'L1_attn_proj_w': 8.0,
     'L1_ffn_w_gate': 8.0,
     'L1_ffn_w_up': 8.0,
     'L1_ffn_w_down': 8.0}
    for name, (base, spread) in spreads.items():
        noise = np.random.default_rng([zlib.crc32(name.encode()), seed]).standard_normal(out[name].shape)
        drawn = base * np.exp(spread * noise) if base else spread * noise
        out[name] = jnp.asarray(drawn.astype(out[name].dtype))
    for name, factor in factors.items():
        out[name] = (out[name] * factor).astype(out[name].dtype)
    return out
```

```python
from contextlib import ExitStack

import numpy as np

import concourse.bass as bass
from concourse import mybir

F32 = mybir.dt.float32
BF16 = mybir.dt.bfloat16
ALU = mybir.AluOpType
ACT = mybir.ActivationFunctionType
AX = mybir.AxisListType

P = 128
D = 128
H = 16
DK = D // H
L = 256
TILE = 128
NT = 4
GROUP = NT * TILE
SEQS = GROUP // L
E = 8
DFF = 512
FC = DFF // P
I2 = 352
BLK = 16
NB_X = D // BLK
NB_H = I2 // BLK
JT = 4
HG = H // JT
SLOTS = 6
MAX_ROW = 96
VW = DK + 1
EPS = 1e-5
RMS_EPS = 1e-6
SCALE = float(DK) ** -0.5
Q_SLOTS = (0, 1, 2, 0, 1, 0)
K_SLOTS = (0, 0, 0, 1, 1, 2)
K_CHUNKS = ((0, 128), (128, 128), (256, 96))

VECS = ["conv_w0", "conv_w1", "conv_w2", "conv_w3", "conv_b", "b_r", "b_i", "log_a", "ln1_g", "ln1_b",
        "b_q", "b_k", "ln2_g", "ln2_b", "qn_w", "qn_b", "kn_w", "kn_b"]
VEC = {n: i for i, n in enumerate(VECS)}
NVEC = len(VECS)
MATS = ["W_r", "W_i", "W_out", "wq", "wk", "wv", "wo", "q1", "k1", "v1", "proj"]
MAT = {n: i for i, n in enumerate(MATS)}
ROWS_BC = ["b_v", "b_o", "gamma", "proj_b"]
ROWI = {n: i for i, n in enumerate(ROWS_BC)}


class Steps:

    def __init__(self, eng, sem, start=0):
        self.eng, self.sem, self.base, self.n = eng, sem, start, 0

    def turn(self, base):
        self.base, self.n = base, 0

    def mark(self, ins):
        self.n += 1
        ins.then_inc(self.sem, 1)

    def sync(self):
        self.eng.wait_ge(self.sem, self.base + self.n)

    def link(self, ins):
        self.mark(ins)
        self.sync()



def tiles(g, n=NT):
    return bass.ds(g * NT, n)


def bc_last(t, n, w):
    return t[:, 0:n].unsqueeze(2).broadcast_to([P, n, w])


class Shared:

    def __init__(self, nc):
        self.nc = nc
        self.count = 0

    def name(self, name):
        self.count += 1
        return f"{name}_{self.count}"

    def sem(self, ctx, name):
        return ctx.enter_context(self.nc.semaphore(self.name(name)))

    def sb(self, ctx, name, shape, dt=F32):
        return ctx.enter_context(self.nc.sbuf_tensor(self.name(name), shape, dt))

    def ps(self, ctx, name, shape, dt=F32):
        return ctx.enter_context(self.nc.psum_tensor(self.name(name), shape, dt))

    def v(self, name):
        i = VEC[name]
        return self.vec[:, i:i + 1]

    def m(self, name):
        return self.mat[:, MAT[name], :]

    def rowbc(self, name, n):
        return self.row[:, ROWI[name], :].unsqueeze(1).broadcast_to([P, n, D])


def build(nc, x, vecs, b1v, mats, w1, w2, b2, gate_w, rows, gate_b, w4, consts, out):
    with ExitStack() as top:
        S = Shared(nc)
        T = x.shape[0]
        S.NG, S.NSEQ, S.NTILE, S.out = T // GROUP, T // L, T // TILE, out
        S.q_scr = [nc.dram_tensor(f"q_scratch{l}", [H, SLOTS, DK, T], BF16).ap() for l in range(2)]
        S.k_scr = [nc.dram_tensor(f"k_scratch{l}", [H, SLOTS, DK, T], BF16).ap() for l in range(2)]
        S.x_all = S.sb(top, "x_all", [P, S.NTILE, D])
        S.y_all = S.sb(top, "y_all", [P, S.NTILE, D])
        S.s_all = S.sb(top, "s_all", [P, S.NTILE, D])
        S.v_all = S.sb(top, "v_all", [P, S.NTILE, H, VW])
        S.vec = S.sb(top, "vec", [P, NVEC])
        S.b1c = S.sb(top, "b1c", [P, E * FC])
        S.mat = S.sb(top, "mat", [P, len(MATS), D])
        S.gw_sb = S.sb(top, "gw_sb", [P, E])
        S.b2_sb = S.sb(top, "b2_sb", [E, D])
        S.w1_sb, S.w2_sb = S.sb(top, "w1", [P, E, DFF]), S.sb(top, "w2", [P, E, FC, D])
        S.row = S.sb(top, "row", [P, len(ROWS_BC), D])
        S.gb_row = S.sb(top, "gb_row", [P, E])
        cst = S.sb(top, "cst", [P, 3, P])
        S.ident, S.center, S.block_mean = (cst[:, i, :] for i in range(3))
        S.ident_b = S.sb(top, "ident_b", [P, P], BF16)
        S.tri = S.sb(top, "tri", [P, E * E])
        S.m_half = S.sb(top, "m_half", [P, 8])
        S.eps_c = S.sb(top, "eps_c", [P, 1])
        S.quarter = S.sb(top, "quarter", [P, 1])
        S.hb_r = S.sb(top, "hb_r", [P, 1])
        S.hb_i = S.sb(top, "hb_i", [P, 1])
        S.c4 = S.sb(top, "c4", [P, 1])
        S.wgu_t = S.sb(top, "wgu_t", [P, 2, I2])
        S.wd_t = S.sb(top, "wd_t", [P, 3, D])
        S.stats_ready = S.sem(top, "stats_ready")
        S.x_in, S.w_in, S.w4_in, S.moe_in = (S.sem(top, n) for n in ("x_in", "w_in", "w4_in", "moe_in"))

        phase_setup(S, x, vecs, b1v, mats, w1, w2, b2, gate_w, rows, gate_b, w4, cst, consts)
        phase_pre0(S)
        phase_attention(S, 0)
        phase_moe(S)
        phase_pre1(S)
        phase_attention(S, 1)
        phase_ffn1(S)


def fp4_scale(dve, st, src, nblk, q, amax, rs):
    b3 = lambda t: t.rearrange("p (b k) -> p b k", k=BLK)
    st.link(dve.tensor_reduce(amax[:, 0:nblk], b3(src), AX.X, ALU.max, apply_absolute_value=True))
    st.link(dve.tensor_scalar(amax[:, 0:nblk], amax[:, 0:nblk], 1.0 / 6.0, 1e-12, ALU.mult, ALU.max))
    st.link(dve.reciprocal(rs[:, 0:nblk], amax[:, 0:nblk]))
    st.link(dve.tensor_tensor(b3(q), b3(src), bc_last(rs, nblk, BLK), ALU.mult))


def fp4_magnitude(dve, st, a, r):
    st.link(dve.tensor_scalar(r, a, 5.0, 2.0, ALU.is_gt, ALU.mult))
    st.link(dve.scalar_tensor_tensor(r, a, 3.5, r, ALU.is_gt, ALU.add))
    st.link(dve.scalar_tensor_tensor(r, a, 2.5, r, ALU.is_gt, ALU.add))
    st.link(dve.tensor_scalar(r, r, 2.0, None, ALU.mult))
    for mid in (1.75, 1.25, 0.75, 0.25):
        st.link(dve.scalar_tensor_tensor(r, a, mid, r, ALU.is_gt, ALU.add))


def fp4_value(dve, st, r, sgn, amax, nblk, q):
    b3 = lambda t: t.rearrange("p (b k) -> p b k", k=BLK)
    st.link(dve.scalar_tensor_tensor(q, r, 0.5, sgn, ALU.mult, ALU.mult))
    st.mark(dve.tensor_tensor(b3(q), b3(q), bc_last(amax, nblk, BLK), ALU.mult))


def phase_setup(S, x, vecs, b1v, mats, w1, w2, b2, gate_w, rows, gate_b, w4, cst, consts):
    nc = S.nc
    NW = 6 * P + I2
    NWB = NW // BLK
    N_LOADS = 9
    with ExitStack() as ctx:
        w4_sb = S.sb(ctx, "w4_sb", [P, NW])
        w4n = S.sb(ctx, "w4n", [P, NW])
        w4a = S.sb(ctx, "w4a", [P, NW])
        w4s = S.sb(ctx, "w4s", [P, NW])
        w4r = S.sb(ctx, "w4r", [P, NW])
        amax = S.sb(ctx, "amax", [P, NWB])
        rsc = S.sb(ctx, "rsc", [P, NWB])
        lna = S.sb(ctx, "lna", [P, 4])
        tp = [S.ps(ctx, f"tp{i}", [P, 512]) for i in range(3)]
        steps_dve, steps_act = S.sem(ctx, "setup_dve"), S.sem(ctx, "setup_act")
        exp_ready, base_ready = S.sem(ctx, "exp_ready"), S.sem(ctx, "base_ready")
        w4_scaled, w4_signs, w4_ready = (S.sem(ctx, n) for n in ("w4_scaled", "w4_signs", "w4_ready"))
        w4_turned, ident_in = S.sem(ctx, "w4_turned"), S.sem(ctx, "ident_in")
        pool_done, moved = S.sem(ctx, "pool_done"), S.sem(ctx, "moved")
        block = ctx.enter_context(nc.Block())

        @block.sync
        def _(sp):
            sp.dma_start(S.vec[:], vecs).then_inc(S.w_in, 16)
            sp.dma_start(w4_sb[:], w4).then_inc(S.w4_in, 16)
            sp.dma_start(cst[:], consts[0:P, :].rearrange("p (i n) -> p i n", n=P)).then_inc(S.w_in, 16)
            sp.dma_start(S.x_all[:], x.rearrange("(t p) c -> p t c", p=P)).then_inc(S.x_in, 16)
            sp.dma_start(S.w1_sb[:], w1).then_inc(S.moe_in, 16)
            sp.dma_start(S.w2_sb[:], w2).then_inc(S.moe_in, 16)
            sp.wait_ge(S.w_in, 16 * N_LOADS)
            sp.wait_ge(S.x_in, 16)

        @block.scalar
        def _(act):
            def bcast(ap, n):
                return ap.rearrange("(o n) -> o n", o=1).broadcast_to([P, n])

            act.dma_start(S.mat[:], mats).then_inc(S.w_in, 16)
            act.dma_start(S.tri[:], consts[P:P + 1, 0:E * E].broadcast_to([P, E * E])).then_inc(S.w_in, 16)
            act.dma_start(S.row[:], bcast(rows, len(ROWS_BC) * D)).then_inc(S.w_in, 16)
            act.dma_start(S.gb_row[:], bcast(gate_b, E)).then_inc(S.w_in, 16)
            act.dma_start(S.b1c[:], b1v).then_inc(S.w_in, 16)
            act.dma_start(S.gw_sb[:], gate_w).then_inc(S.w_in, 16)
            act.dma_start(S.b2_sb[:], b2).then_inc(S.w_in, 16)
            act.wait_ge(S.w_in, 16 * N_LOADS)
            act.activation(lna[:, 0:1], S.v("log_a"), ACT.Exp, scale=-1.0).then_inc(exp_ready, 1)
            act.wait_ge(base_ready, 1)
            st = Steps(act, steps_act)
            st.link(act.activation(lna[:, 3:4], lna[:, 2:3], ACT.Ln))
            st.mark(act.mul(S.c4[:], lna[:, 3:4], 4.0))
            st.mark(act.mul(S.hb_r[:], S.v("b_r"), 0.5))
            st.mark(act.mul(S.hb_i[:], S.v("b_i"), 0.5))
            st.mark(act.copy(S.ident_b[:], S.ident))
            act.wait_ge(w4_scaled, 1)
            act.activation(w4a[:], w4n[:], ACT.Abs).then_inc(w4_signs, 1)
            act.activation(w4s[:], w4n[:], ACT.Sign).then_inc(w4_signs, 1)
            act.wait_ge(w4_turned, 1)
            for i in range(2):
                act.copy(S.wgu_t[:, i, :], tp[i][:, 0:I2]).then_inc(moved, 1)
            for i, (_, n) in enumerate(K_CHUNKS):
                act.copy(S.wd_t[0:n, i, :], tp[2][0:n, i * P:(i + 1) * P]).then_inc(moved, 1)

        @block.gpsimd
        def _(pool):
            pool.memset(S.m_half[:], -0.5).then_inc(pool_done, 1)
            pool.memset(S.eps_c[:], EPS).then_inc(pool_done, 1)
            pool.memset(S.quarter[:], 0.25).then_inc(pool_done, 1)
            pool.memset(S.v_all[:], 1.0).then_inc(pool_done, 1)

        @block.vector
        def _(dve):
            st = Steps(dve, steps_dve)
            dve.wait_ge(exp_ready, 1)
            st.link(dve.tensor_scalar(lna[:, 1:2], lna[:, 0:1], 1.0, None, ALU.add))
            dve.reciprocal(lna[:, 2:3], lna[:, 1:2]).then_inc(base_ready, 1)
            dve.wait_ge(S.w4_in, 16)
            fp4_scale(dve, st, w4_sb[:], NWB, w4n[:], amax, rsc)
            dve.sem_inc(w4_scaled, 1)
            dve.wait_ge(w4_signs, 2)
            fp4_magnitude(dve, st, w4a[:], w4r[:])
            fp4_value(dve, st, w4r[:], w4s[:], amax, NWB, w4n[:])
            st.sync()
            dve.sem_inc(w4_ready, 1)

        @block.tensor
        def _(pe):
            pe.wait_ge(S.w_in, 16 * N_LOADS)
            pe.wait_ge(w4_ready, 1)
            for i in range(2):
                for j, (lo, n) in enumerate(K_CHUNKS):
                    col = (3 * i + j) * P
                    pe.transpose(tp[i][:, lo:lo + n], w4n[0:n, col:col + P], S.ident[0:n, 0:n])
            for j, (lo, n) in enumerate(K_CHUNKS):
                last = pe.transpose(tp[2][0:n, j * P:(j + 1) * P], w4n[:, 6 * P + lo:6 * P + lo + n], S.ident)
            last.then_inc(w4_turned, 1)


def norm_stats(dve, st, src, stats, mv, ve, eps, stats_ready):
    for n in range(NT):
        st.mark(dve.bn_stats(stats[:, n, :], src(n)))
    st.sync()
    dve.sem_inc(stats_ready, 1)
    for n in range(NT):
        st.mark(dve.bn_aggr(mv[:, n, :], stats[:, n, :]))
    st.sync()
    return dve.tensor_scalar(ve[:, 0:NT], mv[:, :, 1], eps, None, ALU.add)


def phase_pre0(S):
    nc = S.nc
    with ExitStack() as ctx:
        sb = lambda n, shape, dt=F32: S.sb(ctx, n, shape, dt)
        sem = lambda n: S.sem(ctx, n)
        stats, mv = sb("stats", [P, NT, 6]), sb("mv", [P, NT, 2])
        ve, rstd = sb("ve", [P, 3, NT]), sb("rstd", [P, 3, NT])
        xn, hn = sb("xn", [P, NT, D]), sb("hn", [P, NT, D])
        xn_t, h1_t = sb("xn_t", [P, GROUP]), sb("h1_t", [P, GROUP])
        xc = sb("xc", [P, SEQS, L])
        tr, ti, a, a2 = (sb(n, [P, GROUP]) for n in ("tr", "ti", "a", "a2"))
        sc, hs = sb("sc", [P, GROUP]), sb("hs", [P, GROUP])
        ssq, junk = sb("ssq", [P, NT]), sb("junk", [P, D])
        parts, rest = sb("parts", [P, 2, 3, GROUP], BF16), sb("rest", [P, 2, GROUP])
        p_xn, p_hn, p_r, p_i, p_q, p_k, p_v, p_s = (S.ps(ctx, n, [P, 512]) for n in
                                                    ("p_xn", "p_hn", "p_r", "p_i", "p_q", "p_k", "p_v", "p_s"))
        steps_dve, steps_act = sem("steps_dve"), sem("steps_act")
        var_ready, rstd_ready = sem("var_ready"), sem("rstd_ready")
        xn_ready, xn_turned, xnt_ready, xn_kept = sem("xn_ready"), sem("xn_turned"), sem("xnt_ready"), sem("xn_kept")
        hn_ready, hn_turned, ht_ready = sem("hn_ready"), sem("hn_turned"), sem("ht_ready")
        qkv_done, conv_ready, gates_done = sem("qkv_done"), sem("conv_ready"), sem("gates_done")
        tanh_ready, a2_ready, clip_ready, sc_ready = sem("tanh_ready"), sem("a2_ready"), sem("clip_ready"), sem("sc_ready")
        hs_ready, s_done, ss_ready = sem("hs_ready"), sem("s_done"), sem("ss_ready")
        part1_ready, rest_ready, part2_ready, parts_ready = (sem(n) for n in ("part1", "rest", "part2", "parts"))
        v_kept, s_kept, stored = sem("v_kept"), sem("s_kept"), sem("stored")
        STORES = 2 * SLOTS
        block = ctx.enter_context(nc.Block())

        @block.sync
        def _(sp):
            sp.sem_inc(stored, 16)
            with sp.Fori(0, S.NG) as g:
                sp.wait_ge(parts_ready, g + 1)
                store_parts(sp, S, 0, g, parts, stored)
            sp.wait_ge(stored, 16 * STORES * S.NG + 16)

        @block.gpsimd
        def _(pool):
            pool.sem_inc(xn_kept, 1)
            with pool.Fori(0, S.NG) as g:
                for k in range(3):
                    pool.wait_ge(var_ready, g * 3 + k + 1)
                    pool.tensor_tensor(rstd[:, k, :], ve[:, k, :], S.m_half[:, 0:NT], ALU.pow).then_inc(rstd_ready, 1)
                    if k == 1:
                        pool.wait_ge(xn_ready, g + 1)
                        pool.tensor_tensor(S.y_all[:, tiles(g), :], xn[:], S.rowbc("b_o", NT), ALU.add
                                           ).then_inc(xn_kept, 1)

        @block.vector
        def _(dve):
            st = Steps(dve, steps_dve)
            PER = 44
            dve.sem_inc(conv_ready, 1)
            dve.sem_inc(hs_ready, 1)
            dve.sem_inc(rest_ready, 1)
            dve.sem_inc(v_kept, 1)
            dve.sem_inc(s_kept, 1)
            with dve.Fori(0, S.NG) as g:
                st.turn(g * PER)
                norm_stats(dve, st, lambda n: S.x_all[:, bass.ds(g * NT + n, 1), :], stats, mv, ve[:, 0, :], EPS, S.stats_ready
                           ).then_inc(var_ready, 1)
                dve.wait_ge(rstd_ready, g * 3 + 1)
                dve.wait_ge(xn_turned, g + 1)
                dve.wait_ge(xn_kept, g + 1)
                for n in range(NT):
                    st.mark(dve.tensor_scalar(xn[:, n, :], S.x_all[:, bass.ds(g * NT + n, 1), :], mv[:, n, 0:1],
                                              rstd[:, 0, n:n + 1], ALU.subtract, ALU.mult))
                st.sync()
                dve.sem_inc(xn_ready, 1)
                norm_stats(dve, st, lambda n: xn[:, n, :], stats, mv, ve[:, 1, :], EPS, S.stats_ready).then_inc(var_ready, 1)
                dve.wait_ge(rstd_ready, g * 3 + 2)
                dve.wait_ge(hn_turned, g + 1)
                for n in range(NT):
                    st.mark(dve.tensor_scalar(hn[:, n, :], xn[:, n, :], mv[:, n, 0:1], rstd[:, 1, n:n + 1],
                                              ALU.subtract, ALU.mult))
                st.sync()
                dve.sem_inc(hn_ready, 1)
                dve.wait_ge(xnt_ready, g + 2)
                dve.wait_ge(gates_done, g + 1)
                x3 = xn_t[:].rearrange("p (s t) -> p s t", t=L)
                st.link(dve.tensor_scalar(xc[:], x3, S.v("conv_w3"), S.v("conv_b"), ALU.mult, ALU.add))
                for back in (1, 2, 3):
                    st.link(dve.scalar_tensor_tensor(xc[:, :, back:], x3[:, :, :L - back], S.v(f"conv_w{3 - back}"),
                                                     xc[:, :, back:], ALU.mult, ALU.add))
                dve.sem_inc(conv_ready, 1)
                dve.wait_ge(part1_ready, g + 1)
                dve.wait_ge(part2_ready, g + 1)
                for i, (ps, bias) in enumerate(((p_q, "b_q"), (p_k, "b_k"))):
                    st.mark(dve.scalar_tensor_tensor(rest[:, i, :], ps[:], S.v(bias), parts[:, i, 0, :],
                                                     ALU.add, ALU.subtract))
                st.sync()
                dve.sem_inc(rest_ready, 1)
                for n in range(NT):
                    st.mark(dve.tensor_tensor(S.v_all[:, bass.ds(g * NT + n, 1), :, 0:DK],
                                              p_v[:, n * D:(n + 1) * D].rearrange("p (h d) -> p h d", d=DK),
                                              S.row[:, ROWI["b_v"], :].rearrange("p (h d) -> p h d", d=DK), ALU.add))
                st.sync()
                dve.sem_inc(v_kept, 1)
                dve.wait_ge(a2_ready, g + 1)
                st.link(dve.tensor_scalar(a2[:], a2[:], 1.0, None, ALU.min))
                dve.sem_inc(clip_ready, 1)
                st.link(dve.scalar_tensor_tensor(ti[:], ti[:], 1.0, xc[:].rearrange("p s t -> p (s t)"),
                                                 ALU.add, ALU.mult))
                dve.wait_ge(part2_ready, g + 2)
                st.link(dve.tensor_tensor(parts[:, :, 2, :], rest[:], parts[:, :, 1, :], ALU.subtract))
                dve.sem_inc(parts_ready, 1)
                dve.wait_ge(sc_ready, g + 1)
                st.link(dve.tensor_tensor(ti[:], ti[:], sc[:], ALU.mult))
                dve.wait_ge(s_done, g + 1)
                for s in range(SEQS):
                    cols = slice(s * L, (s + 1) * L)
                    st.mark(dve.tensor_tensor_scan(hs[:, cols], a[:, cols], ti[:, cols], 0.0, ALU.mult, ALU.add))
                st.sync()
                dve.sem_inc(hs_ready, 1)
                dve.wait_ge(ss_ready, g + 1)
                dve.tensor_scalar(ve[:, 2, :], ssq[:], 1.0 / D, RMS_EPS, ALU.mult, ALU.add).then_inc(var_ready, 1)
                dve.wait_ge(rstd_ready, g * 3 + 3)
                for n in range(NT):
                    st.mark(dve.scalar_tensor_tensor(S.s_all[:, bass.ds(g * NT + n, 1), :], p_s[:, n * D:(n + 1) * D],
                                                     rstd[:, 2, n:n + 1], S.row[:, ROWI["gamma"], :],
                                                     ALU.mult, ALU.mult))
                st.sync()
                dve.sem_inc(s_kept, 1)
                assert st.n == PER, st.n

        @block.scalar
        def _(act):
            st = Steps(act, steps_act)
            PER = 10
            act.sem_inc(part2_ready, 1)
            act.sem_inc(xnt_ready, 1)
            act.sem_inc(ht_ready, 1)
            act.sem_inc(tanh_ready, 1)
            with act.Fori(0, S.NG) as g:
                st.turn(g * PER)
                act.wait_ge(xn_turned, g + 2)
                act.wait_ge(conv_ready, g + 1)
                act.copy(xn_t[:], p_xn[:]).then_inc(xnt_ready, 1)
                act.wait_ge(hn_turned, g + 2)
                act.activation(h1_t[:], p_hn[:], ACT.Identity, bias=S.v("ln1_b"), scale=S.v("ln1_g")
                               ).then_inc(ht_ready, 1)
                act.wait_ge(qkv_done, g + 1)
                act.wait_ge(stored, g * (16 * STORES) + 16)
                st.mark(act.activation(parts[:, 0, 0, :], p_q[:], ACT.Identity, bias=S.v("b_q")))
                st.mark(act.activation(parts[:, 1, 0, :], p_k[:], ACT.Identity, bias=S.v("b_k")))
                st.sync()
                act.sem_inc(part1_ready, 1)
                act.wait_ge(gates_done, g + 2)
                act.wait_ge(hs_ready, g + 1)
                st.mark(act.activation(tr[:], p_r[:], ACT.Tanh, bias=S.hb_r[:], scale=0.5))
                st.mark(act.activation(ti[:], p_i[:], ACT.Tanh, bias=S.hb_i[:], scale=0.5))
                st.sync()
                act.sem_inc(tanh_ready, 1)
                st.link(act.activation(a[:], tr[:], ACT.Exp, bias=S.c4[:], scale=S.c4[:]))
                st.mark(act.activation(a2[:], a[:], ACT.Square))
                st.sync()
                act.sem_inc(a2_ready, 1)
                act.wait_ge(rest_ready, g + 2)
                act.copy(parts[:, :, 1, :], rest[:]).then_inc(part2_ready, 1)
                act.wait_ge(clip_ready, g + 1)
                act.activation(sc[:], a2[:], ACT.Sqrt, bias=S.quarter[:], scale=-0.25).then_inc(sc_ready, 1)
                act.wait_ge(s_done, g + 2)
                for n in range(NT):
                    st.mark(act.activation(junk[:], p_s[:, n * D:(n + 1) * D], ACT.Square,
                                           accum_out=ssq[:, n:n + 1]))
                    st.sync()
                act.sem_inc(ss_ready, 1)
                assert st.n == PER, st.n

        @block.tensor
        def _(pe):
            pe.sem_inc(xn_turned, 1)
            pe.sem_inc(hn_turned, 1)
            pe.sem_inc(gates_done, 1)
            pe.sem_inc(s_done, 1)
            with pe.Fori(0, S.NG) as g:
                pe.wait_ge(xn_ready, g + 1)
                pe.wait_ge(xnt_ready, g + 1)
                for n in range(NT):
                    last = pe.transpose(p_xn[:, n * P:(n + 1) * P], xn[:, n, :], S.ident)
                last.then_inc(xn_turned, 1)
                pe.wait_ge(hn_ready, g + 1)
                pe.wait_ge(ht_ready, g + 1)
                for n in range(NT):
                    last = pe.transpose(p_hn[:, n * P:(n + 1) * P], hn[:, n, :], S.ident)
                last.then_inc(hn_turned, 1)
                pe.wait_ge(ht_ready, g + 2)
                pe.wait_ge(rest_ready, g + 1)
                pe.wait_ge(v_kept, g + 1)
                pe.matmul(p_q[:], S.m("wq"), h1_t[:], start=True, stop=True)
                pe.matmul(p_k[:], S.m("wk"), h1_t[:], start=True, stop=True)
                for n in range(NT):
                    last = pe.matmul(p_v[:, n * D:(n + 1) * D], h1_t[:, n * P:(n + 1) * P], S.m("wv"),
                                     start=True, stop=True)
                last.then_inc(qkv_done, 1)
                pe.wait_ge(conv_ready, g + 2)
                pe.wait_ge(tanh_ready, g + 1)
                xcf = xc[:].rearrange("p s t -> p (s t)")
                pe.matmul(p_r[:], S.m("W_r"), xcf, start=True, stop=True)
                pe.matmul(p_i[:], S.m("W_i"), xcf, start=True, stop=True).then_inc(gates_done, 1)
                pe.wait_ge(hs_ready, g + 2)
                pe.wait_ge(s_kept, g + 1)
                for n in range(NT):
                    last = pe.matmul(p_s[:, n * D:(n + 1) * D], hs[:, n * P:(n + 1) * P], S.m("W_out"),
                                     start=True, stop=True)
                last.then_inc(s_done, 1)


def store_parts(sp, S, layer, g, parts, stored):
    cols = bass.ds(g * GROUP, GROUP)
    for i, (scr, slots) in enumerate(((S.q_scr[layer], Q_SLOTS), (S.k_scr[layer], K_SLOTS))):
        for slot, part in enumerate(slots):
            sp.dma_start(scr[:, slot, :, cols], parts[:, i, part, :]).then_inc(stored, 16)


def phase_attention(S, layer):
    nc = S.nc
    NB = S.NSEQ
    HALF = H // 2
    with ExitStack() as ctx:
        sb = lambda n, shape, dt=F32: S.sb(ctx, n, shape, dt)
        sem = lambda n: S.sem(ctx, n)
        ks = [sb(f"ks{u}", [P, H, L], BF16) for u in range(2)]
        qs = [sb(f"qs{u}", [P, H, L], BF16) for u in range(2)]
        vs = [sb(f"vs{u}", [P, 2, H, VW]) for u in range(2)]
        N_BANK, N_PR = 4, 4
        pr = [sb(f"pr{i}", [P, JT, L]) for i in range(N_PR)]
        neg_max = sb("neg_max", [P, 2, 2, HALF])
        max_rest = sb("max_rest", [P, 2, HALF])
        max_parts = [sb(f"max_parts{i}", [P, 2, 3, HALF], BF16) for i in range(2)]
        max_rows = [sb(f"max_rows{i}", [3 * HALF, L], BF16) for i in range(2)]
        o_raw = sb("o_raw", [P, HG, L])
        o_rec, o_n, o_t = sb("o_rec", [P, 2, H]), sb("o_n", [P, 2, H, DK]), sb("o_t", [P, L])
        bank = [S.ps(ctx, f"bank{i}", [P, 512]) for i in range(N_BANK)]
        score = [S.ps(ctx, f"score{i}", [P, 2, L]) for i in range(2)]
        p_o = S.ps(ctx, "p_o", [P, HG, L])
        k_in, q_in = [sem(f"k_in{u}") for u in range(2)], [sem(f"q_in{u}") for u in range(2)]
        rows_in = [sem("rows_in0"), sem("rows_in1")]
        operands_set, o_set, v_copied = sem("operands_set"), sem("o_set"), sem("v_copied")
        bank_full, bank_free, pr_free = sem("bank_full"), sem("bank_free"), sem("pr_free")
        score_full, exp_done = sem("score_full"), sem("exp_done")
        steps_dve, steps_norm = sem("steps_dve"), sem("steps_norm")
        parts_ready, rows_ready = sem("max_parts"), sem("max_rows")
        turn_started = sem("turn_started")
        o_moved, o_turned, o_ready, ot_ready = sem("o_moved"), sem("o_turned"), sem("o_ready"), sem("ot_ready")
        STEPS = 2 * HG
        block = ctx.enter_context(nc.Block())

        HALVES = 2 * STEPS
        LAG = 1

        AT = {0: [('rows', 1)], 1: [('norm', 0), ('norm', 1)], 2: [('norm', 2)], 3: [('norm', 3)], 4: [('rows', 0)]}

        def plan(s, maxima, norm):
            uses = [("max", h) for h in (2 * s, 2 * s + 1)] if maxima else []
            return uses + [x for x in AT.get(s, []) if x[0] != "norm" and (maxima or x[1] == 1)
                           or x[0] == "norm" and norm]

        FIRST = [("max", h) for h in range(H)]
        FIRST.insert(2 * 4 + 2, ("rows", 0))
        SEQ0 = [x for s in range(STEPS) for x in plan(s, True, False)]
        SEQ = [x for s in range(STEPS) for x in plan(s, True, True)]
        assert 2 * len(SEQ) % N_BANK == 0
        BASE0 = len(FIRST)
        BASE1 = BASE0 + len(SEQ0)

        def base(b, kind):
            return 0 if kind == "first" else BASE0 if kind == "start" else BASE1 + (b - 1) * len(SEQ)

        def bank_of(kind, u, i):
            before = {"first": 0, "start": BASE0, "middle": BASE1 + (1 - u) * len(SEQ), "last": BASE1}[kind]
            return bank[(before + i) % N_BANK]

        def sequences(eng, seq):
            seq(0, 0, "start")
            if NB > 2:
                with eng.Fori(0, (NB - 2) // 2) as pair:
                    seq(pair * 2 + 1, 1, "middle")
                    seq(pair * 2 + 2, 0, "middle")
            seq(NB - 1, 1, "last")

        def steps(kind):
            i = 0
            for s in range(STEPS):
                uses = plan(s, kind != "last", kind != "start")
                yield s, i, uses
                i += len(uses)

        LAST_USES = sum(len(plan(s, False, True)) for s in range(STEPS))

        @block.sync
        def _(sp):
            def load(b, u):
                cols = bass.ds(b * L, L)
                for scr, dst, done in ((S.k_scr[layer], ks[u], k_in[u]), (S.q_scr[layer], qs[u], q_in[u])):
                    sp.dma_start(dst[0:SLOTS * DK], scr[:, :, :, cols].rearrange("h s d t -> (s d) h t")
                                 ).then_inc(done, 16)

            def maxima_to_queries(c, u, half):
                sp.wait_ge(rows_ready, c * 2 + half + 1)
                for p in range(3):
                    row = MAX_ROW + p
                    sp.dma_start(qs[u][row:row + 1, half * HALF:(half + 1) * HALF, :].rearrange("o h t -> o (h t)"),
                                 max_rows[half][p * HALF:(p + 1) * HALF, :]).then_inc(rows_in[half], 16)

            sp.wait_ge(operands_set, 6)
            load(0, 0)
            load(1, 1)
            maxima_to_queries(0, 0, 0)
            maxima_to_queries(0, 0, 1)
            maxima_to_queries(1, 1, 0)
            if NB > 2:
                with sp.Fori(0, (NB - 2) // 2) as pair:
                    for u in range(2):
                        b = pair * 2 + u
                        sp.wait_ge(score_full, (b + 1) * HALVES)
                        load(b + 2, u)
                        maxima_to_queries(b + 1, 1 - u, 1)
                        maxima_to_queries(b + 2, u, 0)
            maxima_to_queries(NB - 1, 1, 1)
            for half in range(2):
                sp.wait_ge(rows_in[half], 48 * NB)

        @block.gpsimd
        def _(pool):
            for u in range(2):
                pool.memset(qs[u][:], 0.0).then_inc(operands_set, 1)

            def copy_v(b, u):
                pool.tensor_copy(vs[u][:], S.v_all[:, bass.ds(2 * b, 2), :, :]).then_inc(v_copied, 1)

            copy_v(0, 0)
            copy_v(1, 1)
            if NB > 2:
                with pool.Fori(0, (NB - 2) // 2) as pair:
                    for u in range(2):
                        b = pair * 2 + u
                        pool.wait_ge(pr_free, (b + 1) * STEPS + N_PR)
                        copy_v(b + 2, u)

        @block.vector
        def _(dve):
            st, sn = Steps(dve, steps_dve), Steps(dve, steps_norm)

            def consume(c, use, bk, what):
                kind, i = what
                if kind == "max":
                    dve.wait_ge(bank_full, use + 1)
                    dve.tensor_reduce(neg_max[:, i // HALF, :, i % HALF:i % HALF + 1],
                                      bk[:].rearrange("p (q t) -> p q t", t=L), AX.X, ALU.max, negate=True
                                      ).then_inc(bank_free, 1)
                    if i % HALF == HALF - 1:
                        split(c, i // HALF, use)
                elif kind == "rows":
                    dve.wait_ge(bank_full, use + 1)
                    if isinstance(c, int) and c == 0:
                        pass
                    else:
                        dve.wait_ge(rows_in[i], 48 * c)
                    dve.tensor_copy(max_rows[i][:], bk[0:3 * HALF, 0:L // 2].bitcast(BF16)).then_inc(bank_free, 1)
                    dve.wait_ge(bank_free, use + 1 + N_BANK)
                    dve.sem_inc(rows_ready, 1)
                else:
                    norm(c, use, bk, i)

            def split(c, half, use):
                st.turn((c * 2 + half) * 4)
                parts = max_parts[half]
                dve.wait_ge(bank_free, use + 1 + N_BANK)
                st.link(dve.tensor_copy(parts[:, :, 0, :], neg_max[:, half]))
                st.link(dve.tensor_tensor(max_rest[:], neg_max[:, half], parts[:, :, 0, :], ALU.subtract))
                st.link(dve.tensor_copy(parts[:, :, 1, :], max_rest[:]))
                st.link(dve.tensor_tensor(parts[:, :, 2, :], max_rest[:], parts[:, :, 1, :], ALU.subtract))
                dve.sem_inc(parts_ready, 1)

            def norm(c, use, bk, stage):
                dve.wait_ge(bank_full, use + 1)
                if stage < 2:
                    sn.turn((c * 2 + stage) * 1)
                    heads = bk[:].rearrange("p (h r) -> p h r", r=32)
                    sn.link(dve.reciprocal(o_rec[:, stage, :].unsqueeze(2), heads[:, :, DK:VW]))
                    dve.tensor_tensor(o_n[:, stage], heads[:, :, 0:DK],
                                      o_rec[:, stage, :].unsqueeze(2).broadcast_to([P, H, DK]), ALU.mult
                                      ).then_inc(bank_free, 1)
                    if stage == 1:
                        dve.wait_ge(bank_free, use + 1 + N_BANK)
                        dve.sem_inc(o_ready, 1)
                elif stage == 2:
                    dve.tensor_copy(o_t[:], bk[:, 0:L]).then_inc(bank_free, 1)
                    dve.wait_ge(bank_free, use + 1 + N_BANK)
                    dve.sem_inc(ot_ready, 1)
                else:
                    proj = bk[:, 0:2 * D].rearrange("p (n c) -> p n c", c=D)
                    two = bass.ds(2 * c, 2)
                    if layer == 0:
                        dve.tensor_tensor(S.y_all[:, two, :], S.y_all[:, two, :], proj, ALU.add
                                          ).then_inc(bank_free, 1)
                    else:
                        dve.tensor_tensor(S.s_all[:, two, :], proj, S.rowbc("proj_b", 2), ALU.add
                                          ).then_inc(bank_free, 1)

            def seq(b, u, kind):
                for s, first, uses in steps(kind):
                    for i, what in enumerate(uses, first):
                        c = b - 1 if what[0] == "norm" else b if what == ("rows", 1) else b + 1
                        consume(c, base(b, kind) + i, bank_of(kind, u, i), what)

            for u in range(2):
                dve.memset(ks[u][0:MAX_ROW], 0.0).then_inc(operands_set, 1)
                dve.memset(ks[u][MAX_ROW:P], 1.0).then_inc(operands_set, 1)
            dve.memset(p_o[:], 0.0).then_inc(o_set, 1)
            dve.sem_inc(bank_free, N_BANK)
            for i, what in enumerate(FIRST):
                consume(0, i, bank_of("first", 0, i), what)
            sequences(dve, seq)
            for stage in range(4):
                i = LAST_USES + stage
                consume(NB - 1, base(NB - 1, "last") + i, bank_of("last", 1, i), ("norm", stage))

        @block.scalar
        def _(act):
            def move_output(b):
                act.wait_ge(pr_free, (b + 1) * STEPS + N_PR)
                act.wait_ge(o_turned, b + 1)
                act.copy(o_raw[:], p_o[:]).then_inc(o_moved, 1)

            def seq(b, u, kind):
                for s in range(STEPS):
                    act.wait_ge(pr_free, b * STEPS + s + 1)
                    for k in range(2):
                        act.wait_ge(score_full, b * HALVES + 2 * s + k + 1)
                        act.activation(pr[s % N_PR][:, 2 * k:2 * k + 2, :], score[k][:], ACT.Exp, scale=SCALE
                                       ).then_inc(exp_done, 1)
                    if s == LAG - 1 and kind != "start":
                        move_output(b - 1)

            act.sem_inc(exp_done, 2)
            act.sem_inc(o_moved, 1)
            sequences(act, seq)
            move_output(NB - 1)

        @block.tensor
        def _(pe):
            def produce(c, u, use, bk, what):
                kind, i = what
                pe.wait_ge(bank_free, use + 1)
                if kind == "max":
                    if i == 0:
                        pe.wait_ge(k_in[u], (c - u) * 8 + 16)
                        pe.wait_ge(q_in[u], (c - u) * 8 + 16)
                    for qt in range(2):
                        last = pe.matmul(bk[:, qt * L:(qt + 1) * L], qs[u][0:MAX_ROW, i, qt * P:(qt + 1) * P],
                                         ks[u][0:MAX_ROW, i, :], start=True, stop=True)
                elif kind == "rows":
                    pe.wait_ge(parts_ready, c * 2 + i + 1)
                    pe.sem_inc(turn_started, 1)
                    turned = bk[0:3 * HALF, 0:L // 2].bitcast(BF16)
                    for qt in range(2):
                        last = pe.transpose(turned[:, qt * P:(qt + 1) * P],
                                            max_parts[i][:, qt, :, :].rearrange("p k h -> p (k h)"), S.ident_b[:])
                elif i < 2:
                    if i == 0:
                        pe.wait_ge(o_moved, c + 2)
                    for hg in range(HG):
                        last = pe.transpose(bk[:, hg * P:(hg + 1) * P], o_raw[:, hg, i * P:(i + 1) * P], S.ident)
                elif i == 2:
                    pe.sem_inc(o_turned, 1)
                    pe.wait_ge(o_ready, c + 1)
                    for qt in range(2):
                        last = pe.transpose(bk[:, qt * P:(qt + 1) * P],
                                            o_n[:, qt].rearrange("p h d -> p (h d)"), S.ident)
                else:
                    pe.wait_ge(ot_ready, c + 1)
                    for qt in range(2):
                        last = pe.matmul(bk[:, qt * D:(qt + 1) * D], o_t[:, qt * P:(qt + 1) * P],
                                         S.m(("wo", "proj")[layer]), start=True, stop=True)
                last.then_inc(bank_full, 1)

            def scores(b, u, s):
                hg, kt = divmod(s, 2)
                if s == 0:
                    pe.wait_ge(rows_in[0], 48 * (b + 1))
                if s == STEPS // 2:
                    pe.wait_ge(rows_in[1], 48 * (b + 1))
                for k in range(2):
                    pe.wait_ge(exp_done, b * HALVES + 2 * s + k + 1)
                    for j in range(2):
                        h = hg * JT + 2 * k + j
                        last = pe.matmul(score[k][:, j, :], ks[u][:, h, kt * P:(kt + 1) * P],
                                         qs[u][:, h, :], start=True, stop=True)
                    last.then_inc(score_full, 1)

            def values(b, u, s):
                hg, kt = divmod(s, 2)
                if s == 0:
                    pe.wait_ge(v_copied, b + 1)
                    pe.wait_ge(o_moved, b + 1)
                pe.wait_ge(exp_done, b * HALVES + 2 * s + 4)
                for j in range(JT):
                    last = pe.matmul(p_o[32 * j:32 * j + VW, hg, :], vs[u][:, kt, hg * JT + j, :],
                                     pr[s % N_PR][:, j, :], start=kt == 0, stop=kt == 1)
                last.then_inc(pr_free, 1)

            def seq(b, u, kind):
                for s, first, uses in steps(kind):
                    scores(b, u, s)
                    for i, what in enumerate(uses, first):
                        c = b - 1 if what[0] == "norm" else b if what == ("rows", 1) else b + 1
                        produce(c, 1 - u, base(b, kind) + i, bank_of(kind, u, i), what)
                    if s >= LAG:
                        values(b, u, s - LAG)
                    elif kind != "start":
                        values(b - 1, 1 - u, STEPS + s - LAG)

            pe.sem_inc(pr_free, N_PR)
            pe.sem_inc(o_turned, 1)
            pe.wait_ge(o_set, 1)
            for i, what in enumerate(FIRST):
                produce(0, 0, i, bank_of("first", 0, i), what)
            sequences(pe, seq)
            for s in range(STEPS - LAG, STEPS):
                values(NB - 1, 1, s)
            for stage in range(4):
                i = LAST_USES + stage
                produce(NB - 1, 1, base(NB - 1, "last") + i, bank_of("last", 1, i), ("norm", stage))


def phase_moe(S):
    nc = S.nc
    NG = S.NG
    with ExitStack() as ctx:
        sb = lambda n, shape, dt=F32: S.sb(ctx, n, shape, dt)
        sem = lambda n: S.sem(ctx, n)
        stats, mv = sb("stats", [P, NT, 6]), sb("mv", [P, NT, 2])
        ve, rstd = sb("ve", [P, NT]), sb("rstd", [P, NT])
        hn = sb("hn", [P, NT, D])
        h2_t = [sb(f"h2_t{u}", [P, GROUP]) for u in range(2)]
        lg, top, ex = sb("lg", [P, NT, E]), sb("top", [P, NT]), sb("ex", [P, NT, E])
        gt, eq = sb("gt", [P, NT, E * E]), sb("eq", [P, NT, E * E])
        rank, den = sb("rank", [P, NT, E]), sb("den", [P, NT])
        ew = [sb(f"ew{u}", [P, NT, E]) for u in range(2)]
        ewt = sb("ewt", [E, GROUP])
        N_H, N_HID = 4, 2 * FC
        hid = [sb(f"hid{i}", [P, GROUP]) for i in range(N_HID)]
        acc = [sb(f"acc{u}", [P, NT, D]) for u in range(2)]
        th, zg = sb("th", [P, NT, D]), sb("zg", [P, NT, D])
        p_h = [S.ps(ctx, f"p_h{i}", [P, GROUP]) for i in range(N_H)]
        p_y = [S.ps(ctx, f"p_y{i}", [P, NT, D]) for i in range(2)]
        p_t, p_m = (S.ps(ctx, n, [P, GROUP]) for n in ("p_t", "p_m"))
        steps_dve, steps_gate = sem("steps_dve"), sem("steps_gate")
        var_ready, rstd_ready, hn_ready, hn_turned, ht_ready = (
            sem(n) for n in ("var_ready", "rstd_ready", "hn_ready", "hn_turned", "ht_ready"))
        logits_done, shifted, exp_ready, ew_ready, ew_turned, ewt_ready, b2_done, acc_set = (
            sem(n) for n in ("logits_done", "shifted", "exp_ready", "ew_ready", "ew_turned", "ewt_ready", "b2_done",
                             "acc_set"))
        h_full, hid_full, y_full, y_free = sem("h_full"), sem("hid_full"), sem("y_full"), sem("y_free")
        acc_done, tanh_ready = sem("acc_done"), sem("tanh_ready")
        CHUNKS = E * FC
        block = ctx.enter_context(nc.Block())

        def groups(eng, group):
            if NG > 2:
                with eng.Fori(0, (NG - 2) // 2) as pair:
                    i = pair * 2
                    group(i, 0, True)
                    group(i + 1, 1, True)
            group(NG - 2, 0, True)
            group(NG - 1, 1, False)

        @block.gpsimd
        def _(pool):
            with pool.Fori(0, NG) as g:
                pool.wait_ge(var_ready, g + 1)
                pool.tensor_tensor(rstd[:], ve[:], S.m_half[:, 0:NT], ALU.pow).then_inc(rstd_ready, 1)

        @block.vector
        def _(dve):
            st, sg = Steps(dve, steps_dve), Steps(dve, steps_gate)
            PER_NORM, PER_ROUTE = 12, 17

            def norm(g, u):
                st.turn(g * (PER_NORM + PER_ROUTE))
                norm_stats(dve, st, lambda n: S.y_all[:, bass.ds(g * NT + n, 1), :], stats, mv, ve, EPS, S.stats_ready
                           ).then_inc(var_ready, 1)
                dve.wait_ge(rstd_ready, g + 1)
                dve.wait_ge(hn_turned, g)
                for n in range(NT):
                    st.mark(dve.tensor_scalar(hn[:, n, :], S.y_all[:, bass.ds(g * NT + n, 1), :], mv[:, n, 0:1],
                                              rstd[:, n:n + 1], ALU.subtract, ALU.mult))
                st.sync()
                dve.sem_inc(hn_ready, 1)
                assert st.n == PER_NORM, st.n

            def route(g, u):
                dve.wait_ge(logits_done, g + 1)
                st.link(dve.tensor_tensor(lg[:], p_m[:, 0:NT * E].rearrange("p (n e) -> p n e", e=E),
                                          S.gb_row[:].unsqueeze(1).broadcast_to([P, NT, E]), ALU.add))
                st.link(dve.tensor_reduce(top[:], lg[:], AX.X, ALU.max))
                st.link(dve.tensor_tensor(ex[:], lg[:], bc_last(top, NT, E), ALU.subtract))
                dve.sem_inc(shifted, 1)
                for n in range(NT):
                    other = lg[:, n, :].unsqueeze(1).broadcast_to([P, E, E])
                    own = lg[:, n, :].unsqueeze(2).broadcast_to([P, E, E])
                    grid = lambda t: t[:, n, :].rearrange("p (i j) -> p i j", j=E)
                    st.mark(dve.tensor_tensor(grid(gt), other, own, ALU.is_gt))
                    st.mark(dve.tensor_tensor(grid(eq), other, own, ALU.is_equal))
                st.sync()
                st.link(dve.tensor_tensor(eq[:], eq[:], S.tri[:].unsqueeze(1).broadcast_to([P, NT, E * E]), ALU.mult))
                st.link(dve.tensor_tensor(gt[:], gt[:], eq[:], ALU.add))
                st.link(dve.tensor_reduce(rank[:], gt[:].rearrange("p n (i j) -> p n i j", j=E), AX.X, ALU.add))
                dve.wait_ge(exp_ready, g + 1)
                st.link(dve.scalar_tensor_tensor(ex[:], rank[:], 2.0, ex[:], ALU.is_lt, ALU.mult))
                st.link(dve.tensor_reduce(den[:], ex[:], AX.X, ALU.add))
                st.link(dve.reciprocal(den[:], den[:]))
                dve.tensor_tensor(ew[u][:], ex[:], bc_last(den, NT, E), ALU.mult).then_inc(ew_ready, 1)
                assert st.n == PER_NORM + PER_ROUTE, st.n

            def start_acc(g, u):
                dve.wait_ge(b2_done, g + 1)
                dve.tensor_tensor(acc[u][:], S.y_all[:, tiles(g), :], p_t[:].rearrange("p (n c) -> p n c", c=D),
                                  ALU.add).then_inc(acc_set, 1)

            def group(g, u, more):
                for e in range(E):
                    if more and e == 0:
                        norm(g + 1, 1 - u)
                    if more and e == 3:
                        route(g + 1, 1 - u)
                    if more and e == 7:
                        start_acc(g + 1, 1 - u)
                    dve.wait_ge(y_full, g * E + e + 3)
                    if e == 0:
                        dve.wait_ge(acc_set, g + 1)
                        dve.wait_ge(ew_ready, g + 1)
                    else:
                        dve.wait_ge(y_free, (g * E + e) * NT + 2 * NT)
                    for n in range(NT):
                        dve.scalar_tensor_tensor(acc[u][:, n, :], p_y[e % 2][:, n, :], ew[u][:, n, e:e + 1],
                                                 acc[u][:, n, :], ALU.mult, ALU.add).then_inc(y_free, 1)
                sg.turn(g * 3)
                dve.wait_ge(y_free, (g + 1) * E * NT + 2 * NT)
                dve.sem_inc(acc_done, 1)
                dve.wait_ge(tanh_ready, g + 1)
                sg.link(dve.scalar_tensor_tensor(zg[:], th[:], 1.0, acc[u][:], ALU.add, ALU.mult))
                sg.link(dve.scalar_tensor_tensor(zg[:], zg[:], 0.5, S.s_all[:, tiles(g), :], ALU.mult, ALU.mult))
                sg.mark(dve.tensor_tensor(S.x_all[:, tiles(g), :], S.x_all[:, tiles(g), :], zg[:], ALU.add))

            dve.sem_inc(y_free, 2 * NT)
            norm(0, 0)
            route(0, 0)
            start_acc(0, 0)
            groups(dve, group)

        @block.scalar
        def _(act):
            def norm(g, u):
                act.wait_ge(hn_turned, g + 1)
                act.activation(h2_t[u][:], p_t[:], ACT.Identity, bias=S.v("ln2_b"), scale=S.v("ln2_g")
                               ).then_inc(ht_ready, 1)

            def route(g, u):
                act.wait_ge(shifted, g + 1)
                act.activation(ex[:], ex[:], ACT.Exp).then_inc(exp_ready, 1)

            def turn_weights(g, u):
                act.wait_ge(ew_turned, g + 1)
                act.wait_ge(b2_done, g)
                act.copy(ewt[:], p_m[0:E, :]).then_inc(ewt_ready, 1)

            def group(g, u, more):
                for k in range(CHUNKS):
                    if more and k == 8:
                        norm(g + 1, 1 - u)
                    if more and k == 20:
                        route(g + 1, 1 - u)
                    if more and k == 26:
                        turn_weights(g + 1, 1 - u)
                    act.wait_ge(h_full, g * CHUNKS + k + 1)
                    if k % FC == 0:
                        act.wait_ge(y_full, g * E + k // FC + 1)
                    act.activation(hid[k % N_HID][:], p_h[k % N_H][:], ACT.Relu, bias=S.b1c[:, k:k + 1]
                                   ).then_inc(hid_full, 1)
                act.wait_ge(acc_done, g + 1)
                act.activation(th[:], acc[u][:], ACT.Tanh, scale=0.5).then_inc(tanh_ready, 1)

            act.sem_inc(hid_full, N_H)
            norm(0, 0)
            route(0, 0)
            turn_weights(0, 0)
            groups(act, group)

        @block.tensor
        def _(pe):
            def norm(g, u):
                pe.wait_ge(hn_ready, g + 1)
                pe.wait_ge(acc_set, g)
                for n in range(NT):
                    last = pe.transpose(p_t[:, n * P:(n + 1) * P], hn[:, n, :], S.ident)
                last.then_inc(hn_turned, 1)

            def logits(g, u):
                pe.wait_ge(ht_ready, g + 1)
                pe.wait_ge(ewt_ready, g)
                for n in range(NT):
                    last = pe.matmul(p_m[:, n * E:(n + 1) * E], h2_t[u][:, n * P:(n + 1) * P], S.gw_sb[:],
                                     start=True, stop=True)
                last.then_inc(logits_done, 1)

            def turn_weights(g, u):
                pe.wait_ge(ew_ready, g + 1)
                for n in range(NT):
                    last = pe.transpose(p_m[0:E, n * P:(n + 1) * P], ew[u][:, n, :], S.ident)
                last.then_inc(ew_turned, 1)

            def bias2(g, u):
                pe.wait_ge(ewt_ready, g + 1)
                for n in range(NT):
                    last = pe.matmul(p_t[:, n * D:(n + 1) * D], ewt[:, n * P:(n + 1) * P], S.b2_sb[:],
                                     start=True, stop=True)
                last.then_inc(b2_done, 1)

            def second(g, e):
                pe.wait_ge(hid_full, (g * E + e + 1) * FC + N_H)
                pe.wait_ge(y_free, (g * E + e + 1) * NT)
                for n in range(NT):
                    for f in range(FC):
                        last = pe.matmul(p_y[e % 2][:, n, :], hid[(e * FC + f) % N_HID][:, n * P:(n + 1) * P],
                                         S.w2_sb[:, e, f, :], start=f == 0, stop=f == FC - 1)
                last.then_inc(y_full, 1)

            def group(g, u, more):
                for k in range(CHUNKS):
                    e, f = divmod(k, FC)
                    if more:
                        for at, stage in ((6, norm), (10, logits), (24, turn_weights), (28, bias2)):
                            if k == at:
                                stage(g + 1, 1 - u)
                    pe.wait_ge(hid_full, g * CHUNKS + k + 1)
                    pe.matmul(p_h[k % N_H][:], S.w1_sb[:, e, f * P:(f + 1) * P], h2_t[u][:],
                              start=True, stop=True).then_inc(h_full, 1)
                    if f == FC - 1 and e > 0:
                        second(g, e - 1)
                second(g, E - 1)

            pe.sem_inc(y_full, 2)
            pe.wait_ge(S.moe_in, 32)
            norm(0, 0)
            logits(0, 0)
            turn_weights(0, 0)
            bias2(0, 0)
            groups(pe, group)


def phase_pre1(S):
    nc = S.nc
    NG = S.NG
    with ExitStack() as ctx:
        sb = lambda n, shape, dt=F32: S.sb(ctx, n, shape, dt)
        sem = lambda n: S.sem(ctx, n)
        stats, mv = sb("stats", [P, NT, 6]), sb("mv", [P, NT, 2])
        ve, rstd = sb("ve", [P, NT]), sb("rstd", [P, NT])
        xn, xn_t = sb("xn", [P, NT, D]), sb("xn_t", [P, GROUP])
        raw, cen, sq, std, nrm = (sb(n, [P, 2, GROUP]) for n in ("raw", "cen", "sq", "std", "nrm"))
        k_sum, k_mean = sb("k_sum", [P, SEQS]), sb("k_mean", [P, SEQS])
        parts, rest = sb("parts", [P, 2, 3, GROUP], BF16), sb("rest", [P, 2, GROUP])
        p_x, p_v = S.ps(ctx, "p_x", [P, 512]), S.ps(ctx, "p_v", [P, 512])
        p_raw, p_cen, p_var = (S.ps(ctx, n, [P, 2, GROUP]) for n in ("p_raw", "p_cen", "p_var"))
        steps_dve, steps_act = sem("steps_dve"), sem("steps_act")
        var_ready, rstd_ready, xn_ready, xn_turned, xt_ready, xn_kept = (
            sem(n) for n in ("var_ready", "rstd_ready", "xn_ready", "xn_turned", "xt_ready", "xn_kept"))
        qkv_done, raw_ready, cen_done, cen_ready, sq_ready, var_done, std_ready = (
            sem(n) for n in ("qkv_done", "raw_ready", "cen_done", "cen_ready", "sq_ready", "var_done", "std_ready"))
        normed, mean_ready, part1_ready, rest_ready, part2_ready, parts_ready, stored, v_kept = (
            sem(n) for n in ("normed", "mean_ready", "part1", "rest", "part2", "parts", "stored", "v_kept"))
        STORES = 2 * SLOTS
        block = ctx.enter_context(nc.Block())

        @block.sync
        def _(sp):
            sp.sem_inc(stored, 16)
            with sp.Fori(0, NG) as g:
                sp.wait_ge(parts_ready, g + 1)
                store_parts(sp, S, 1, g, parts, stored)
            sp.wait_ge(stored, 16 * STORES * NG + 16)

        @block.gpsimd
        def _(pool):
            with pool.Fori(0, NG) as g:
                pool.wait_ge(var_ready, g + 1)
                pool.tensor_tensor(rstd[:], ve[:], S.m_half[:, 0:NT], ALU.pow).then_inc(rstd_ready, 1)

        @block.vector
        def _(dve):
            st = Steps(dve, steps_dve)
            PER = 26
            dve.sem_inc(normed, 1)
            dve.sem_inc(v_kept, 1)
            with dve.Fori(0, NG) as g:
                st.turn(g * PER)
                norm_stats(dve, st, lambda n: S.x_all[:, bass.ds(g * NT + n, 1), :], stats, mv, ve, EPS, S.stats_ready
                           ).then_inc(var_ready, 1)
                dve.wait_ge(rstd_ready, g + 1)
                dve.wait_ge(xn_turned, g + 1)
                dve.wait_ge(xn_kept, g + 1)
                for n in range(NT):
                    st.mark(dve.tensor_scalar(xn[:, n, :], S.x_all[:, bass.ds(g * NT + n, 1), :], mv[:, n, 0:1],
                                              rstd[:, n:n + 1], ALU.subtract, ALU.mult))
                st.sync()
                dve.sem_inc(xn_ready, 1)
                dve.wait_ge(qkv_done, g + 1)
                for n in range(NT):
                    st.mark(dve.tensor_copy(S.v_all[:, bass.ds(g * NT + n, 1), :, 0:DK],
                                            p_v[:, n * D:(n + 1) * D].rearrange("p (h d) -> p h d", d=DK)))
                st.sync()
                dve.sem_inc(v_kept, 1)
                dve.wait_ge(std_ready, g + 2)
                st.link(dve.reciprocal(std[:], std[:]))
                for i, name in enumerate(("qn", "kn")):
                    st.mark(dve.scalar_tensor_tensor(nrm[:, i, :], cen[:, i, :], S.v(name + "_w"), std[:, i, :],
                                                     ALU.mult, ALU.mult))
                st.sync()
                for i, name in enumerate(("qn", "kn")):
                    st.mark(dve.tensor_scalar(nrm[:, i, :], nrm[:, i, :], S.v(name + "_b"), None, ALU.add))
                st.sync()
                k3 = nrm[:, 1, :].rearrange("p (s t) -> p s t", t=L)
                st.link(dve.tensor_reduce(k_sum[:], k3, AX.X, ALU.add))
                st.link(dve.tensor_scalar(k_mean[:], k_sum[:], 1.0 / L, None, ALU.mult))
                st.link(dve.tensor_tensor(k3, k3, bc_last(k_mean, SEQS, L), ALU.subtract))
                dve.sem_inc(normed, 1)
                dve.wait_ge(part1_ready, g + 1)
                st.link(dve.tensor_tensor(rest[:], nrm[:], parts[:, :, 0, :], ALU.subtract))
                dve.sem_inc(rest_ready, 1)
                dve.wait_ge(part2_ready, g + 1)
                st.link(dve.tensor_tensor(parts[:, :, 2, :], rest[:], parts[:, :, 1, :], ALU.subtract))
                dve.sem_inc(parts_ready, 1)
                assert st.n == PER, st.n

        @block.scalar
        def _(act):
            act.sem_inc(xn_kept, 1)
            act.sem_inc(xt_ready, 1)
            act.sem_inc(raw_ready, 1)
            act.sem_inc(sq_ready, 1)
            act.sem_inc(std_ready, 1)
            with act.Fori(0, NG) as g:
                act.wait_ge(xn_turned, g + 2)
                act.copy(xn_t[:], p_x[:]).then_inc(xt_ready, 1)
                act.copy(S.y_all[:, tiles(g), :], xn[:]).then_inc(xn_kept, 1)
                act.wait_ge(qkv_done, g + 1)
                act.wait_ge(cen_done, g + 1)
                act.copy(raw[:], p_raw[:]).then_inc(raw_ready, 1)
                act.wait_ge(cen_done, g + 2)
                act.wait_ge(normed, g + 1)
                act.copy(cen[:], p_cen[:]).then_inc(cen_ready, 1)
                act.wait_ge(var_done, g + 1)
                act.activation(sq[:], p_cen[:], ACT.Square).then_inc(sq_ready, 1)
                act.wait_ge(var_done, g + 2)
                act.activation(std[:], p_var[:], ACT.Sqrt, bias=S.eps_c[:]).then_inc(std_ready, 1)
                act.wait_ge(normed, g + 2)
                act.wait_ge(stored, g * (16 * STORES) + 16)
                act.copy(parts[:, :, 0, :], nrm[:]).then_inc(part1_ready, 1)
                act.wait_ge(rest_ready, g + 1)
                act.copy(parts[:, :, 1, :], rest[:]).then_inc(part2_ready, 1)

        @block.tensor
        def _(pe):
            pe.sem_inc(xn_turned, 1)
            pe.sem_inc(cen_done, 1)
            pe.sem_inc(var_done, 1)
            with pe.Fori(0, NG) as g:
                pe.wait_ge(xn_ready, g + 1)
                pe.wait_ge(xt_ready, g + 1)
                for n in range(NT):
                    last = pe.transpose(p_x[:, n * P:(n + 1) * P], xn[:, n, :], S.ident)
                last.then_inc(xn_turned, 1)
                pe.wait_ge(xt_ready, g + 2)
                pe.wait_ge(raw_ready, g + 1)
                pe.wait_ge(v_kept, g + 1)
                pe.matmul(p_raw[:, 0, :], S.m("q1"), xn_t[:], start=True, stop=True)
                pe.matmul(p_raw[:, 1, :], S.m("k1"), xn_t[:], start=True, stop=True)
                for n in range(NT):
                    last = pe.matmul(p_v[:, n * D:(n + 1) * D], xn_t[:, n * P:(n + 1) * P], S.m("v1"),
                                     start=True, stop=True)
                last.then_inc(qkv_done, 1)
                pe.wait_ge(raw_ready, g + 2)
                pe.wait_ge(sq_ready, g + 1)
                for i in range(2):
                    last = pe.matmul(p_cen[:, i, :], S.center, raw[:, i, :], start=True, stop=True)
                last.then_inc(cen_done, 1)
                pe.wait_ge(sq_ready, g + 2)
                pe.wait_ge(std_ready, g + 1)
                for i in range(2):
                    last = pe.matmul(p_var[:, i, :], S.block_mean, sq[:, i, :], start=True, stop=True)
                last.then_inc(var_done, 1)


def phase_ffn1(S):
    nc = S.nc
    NG = S.NG
    with ExitStack() as ctx:
        sb = lambda n, shape, dt=F32: S.sb(ctx, n, shape, dt)
        sem = lambda n: S.sem(ctx, n)
        NX, NH = GROUP // BLK, NT * NB_H
        xs, xa, xg, xr, xq = (sb(n, [P, GROUP]) for n in ("xs", "xa", "xg", "xr", "xq"))
        amax, rsc = sb("amax", [P, NH]), sb("rsc", [P, NH])
        xq_t = sb("xq_t", [P, GROUP])
        hw = NT * I2
        hv, hsc, ha, hg_, hr, hq = (sb(n, [P, hw]) for n in ("hv", "hsc", "ha", "hg", "hr", "hq"))
        th, gate = sb("th", [P, hw]), sb("gate", [P, hw])
        hq_t = sb("hq_t", [P, 3, GROUP])
        tz, z, o = sb("tz", [P, GROUP]), sb("z", [P, GROUP]), [sb(f"o{u}", [P, NT, D]) for u in range(2)]
        p_gu = [[S.ps(ctx, f"p_gu{i}{j}", [P, 512]) for j in range(2)] for i in range(2)]
        p_t = [S.ps(ctx, f"p_t{i}", [P, 512]) for i in range(3)]
        p_z = S.ps(ctx, "p_z", [P, 512])
        steps_dve, steps_act = sem("steps_dve"), sem("steps_act")
        names = ("x_scaled", "x_signs", "xq_ready", "xq_turned", "xt_ready", "gu_full", "th_ready", "gu_free",
                 "h_scaled", "h_signs", "hq_ready", "hq_turned", "ht_ready", "z_done", "tz_ready", "out_ready",
                 "stored", "z_kept")
        (x_scaled, x_signs, xq_ready, xq_turned, xt_ready, gu_full, th_ready, gu_free, h_scaled, h_signs, hq_ready,
         hq_turned, ht_ready, z_done, tz_ready, out_ready, stored, z_kept) = (sem(n) for n in names)
        block = ctx.enter_context(nc.Block())
        out_v = S.out.rearrange("(t p) c -> p t c", p=P)

        @block.sync
        def _(sp):
            sp.sem_inc(stored, 16)
            with sp.Fori(0, NG) as g:
                sp.wait_ge(out_ready, g + 1)
                sp.dma_start(out_v[:, tiles(g), :], o[0][:]).then_inc(stored, 16)
            sp.wait_ge(stored, 16 * NG + 16)

        @block.vector
        def _(dve):
            st = Steps(dve, steps_dve)
            PER = 39
            dve.sem_inc(z_kept, 1)
            with dve.Fori(0, NG) as g:
                st.turn(g * PER)
                src = S.y_all[:, tiles(g), :].rearrange("p n c -> p (n c)")
                fp4_scale(dve, st, src, NX, xs[:], amax, rsc)
                dve.sem_inc(x_scaled, 1)
                dve.wait_ge(x_signs, g * 2 + 2)
                fp4_magnitude(dve, st, xa[:], xr[:])
                dve.wait_ge(xq_turned, g + 1)
                fp4_value(dve, st, xr[:], xg[:], amax, NX, xq[:])
                st.sync()
                dve.sem_inc(xq_ready, 1)
                for n in range(NT):
                    dve.wait_ge(th_ready, g * NT + n + 1)
                    cols = slice(n * I2, (n + 1) * I2)
                    st.link(dve.scalar_tensor_tensor(gate[:, cols], th[:, cols], 1.0, p_gu[n % 2][0][:, 0:I2],
                                                     ALU.add, ALU.mult))
                    st.link(dve.scalar_tensor_tensor(hv[:, cols], gate[:, cols], 0.5, p_gu[n % 2][1][:, 0:I2],
                                                     ALU.mult, ALU.mult))
                    dve.sem_inc(gu_free, 1)
                fp4_scale(dve, st, hv[:], NH, hsc[:], amax, rsc)
                dve.sem_inc(h_scaled, 1)
                dve.wait_ge(h_signs, g * 2 + 2)
                fp4_magnitude(dve, st, ha[:], hr[:])
                dve.wait_ge(hq_turned, g + 1)
                fp4_value(dve, st, hr[:], hg_[:], amax, NH, hq[:])
                st.sync()
                dve.sem_inc(hq_ready, 1)
                dve.wait_ge(tz_ready, g + 1)
                dve.wait_ge(stored, g * 16 + 16)
                st.link(dve.scalar_tensor_tensor(z[:], tz[:], 1.0, p_z[:], ALU.add, ALU.mult))
                dve.sem_inc(z_kept, 1)
                z3 = z[:].rearrange("p (n c) -> p n c", c=D)
                st.link(dve.scalar_tensor_tensor(z3, z3, 0.5, S.s_all[:, tiles(g), :], ALU.mult, ALU.mult))
                st.link(dve.tensor_tensor(o[0][:], z3, S.x_all[:, tiles(g), :], ALU.add))
                dve.sem_inc(out_ready, 1)
                assert st.n == PER, st.n

        @block.scalar
        def _(act):
            act.sem_inc(ht_ready, 1)
            with act.Fori(0, NG) as g:
                act.wait_ge(x_scaled, g + 1)
                act.activation(xa[:], xs[:], ACT.Abs).then_inc(x_signs, 1)
                act.activation(xg[:], xs[:], ACT.Sign).then_inc(x_signs, 1)
                act.wait_ge(xq_turned, g + 2)
                act.copy(xq_t[:], p_t[0][:]).then_inc(xt_ready, 1)
                for n in range(NT):
                    act.wait_ge(gu_full, g * NT + n + 1)
                    act.activation(th[:, n * I2:(n + 1) * I2], p_gu[n % 2][0][:, 0:I2], ACT.Tanh, scale=0.5
                                   ).then_inc(th_ready, 1)
                act.wait_ge(h_scaled, g + 1)
                act.activation(ha[:], hsc[:], ACT.Abs).then_inc(h_signs, 1)
                act.activation(hg_[:], hsc[:], ACT.Sign).then_inc(h_signs, 1)
                act.wait_ge(hq_turned, g + 2)
                for i, (_, n) in enumerate(K_CHUNKS):
                    act.copy(hq_t[0:n, i, :], p_t[i][0:n, :]).then_inc(ht_ready, 1)
                act.wait_ge(z_done, g + 1)
                act.activation(tz[:], p_z[:], ACT.Tanh, scale=0.5).then_inc(tz_ready, 1)

        @block.tensor
        def _(pe):
            pe.sem_inc(gu_free, 2)
            pe.sem_inc(xq_turned, 1)
            pe.sem_inc(hq_turned, 1)
            with pe.Fori(0, NG) as g:
                pe.wait_ge(xq_ready, g + 1)
                pe.wait_ge(ht_ready, g * 3 + 1)
                for n in range(NT):
                    last = pe.transpose(p_t[0][:, n * P:(n + 1) * P], xq[:, n * P:(n + 1) * P], S.ident)
                last.then_inc(xq_turned, 1)
                pe.wait_ge(xt_ready, g + 1)
                for n in range(NT):
                    pe.wait_ge(gu_free, g * NT + n + 1)
                    for i in range(2):
                        last = pe.matmul(p_gu[n % 2][i][:, 0:I2], xq_t[:, n * P:(n + 1) * P], S.wgu_t[:, i, :],
                                         start=True, stop=True)
                    last.then_inc(gu_full, 1)
                pe.wait_ge(hq_ready, g + 1)
                for n in range(NT):
                    for i, (lo, w) in enumerate(K_CHUNKS):
                        last = pe.transpose(p_t[i][0:w, n * P:(n + 1) * P], hq[:, n * I2 + lo:n * I2 + lo + w],
                                            S.ident)
                last.then_inc(hq_turned, 1)
                pe.wait_ge(ht_ready, g * 3 + 4)
                pe.wait_ge(z_kept, g + 1)
                for n in range(NT):
                    for i, (_, w) in enumerate(K_CHUNKS):
                        last = pe.matmul(p_z[:, n * D:(n + 1) * D], hq_t[0:w, i, n * P:(n + 1) * P],
                                         S.wd_t[0:w, i, :], start=i == 0, stop=i == len(K_CHUNKS) - 1)
                last.then_inc(z_done, 1)


_OUT = "out_dram"


def layout(inputs):
    a = {n: np.asarray(x) for n, x in inputs.items()}
    L0, F0, L1, F1 = "L0_attn_", "L0_ffn_", "L1_attn_", "L1_ffn_"
    x = np.ascontiguousarray(a[L0 + "x"]).reshape(-1, D)
    cw = a[L0 + "conv_w"].reshape(D, 4)
    heads = lambda t: np.tile(t, H)
    vecs = np.stack([cw[:, 0], cw[:, 1], cw[:, 2], cw[:, 3], a[L0 + "conv_b"], a[L0 + "b_r"], a[L0 + "b_i"],
                     a[L0 + "log_a"], a[F0 + "ln1_g"], a[F0 + "ln1_b"], a[F0 + "b_qkv"][0:D],
                     a[F0 + "b_qkv"][D:2 * D], a[F0 + "ln2_g"], a[F0 + "ln2_b"], heads(a[L1 + "q_norm_w"]),
                     heads(a[L1 + "q_norm_b"]), heads(a[L1 + "k_norm_w"]), heads(a[L1 + "k_norm_b"])], axis=1)
    wqkv, qkv1 = a[F0 + "w_qkv"], a[L1 + "qkv_w"].T
    mats = np.stack([a[L0 + "W_r"].T, a[L0 + "W_i"].T, a[L0 + "W_out"].T, wqkv[:, 0:D], wqkv[:, D:2 * D],
                     wqkv[:, 2 * D:], a[F0 + "w_o"], qkv1[:, 0:D], qkv1[:, D:2 * D], qkv1[:, 2 * D:],
                     a[L1 + "proj_w"].T], axis=1)

    def by_rows(w):
        t = np.zeros((3 * P, D), np.float32)
        t[0:I2] = w
        return t.reshape(3, P, D).transpose(1, 0, 2).reshape(P, 3 * D)

    w4 = np.concatenate([by_rows(a[F1 + "w_gate"]), by_rows(a[F1 + "w_up"]), a[F1 + "w_down"]], axis=1)
    w1 = a[F0 + "W1"].transpose(1, 0, 2)
    w2 = a[F0 + "W2"].reshape(E, FC, P, D).transpose(2, 0, 1, 3)
    b1 = a[F0 + "b1"].reshape(E * FC, P).T
    rows = np.concatenate([a[F0 + "b_qkv"][2 * D:], a[F0 + "b_o"], a[L0 + "gamma"], a[L1 + "proj_b"]])
    eye = np.eye(P, dtype=np.float32)
    block = np.kron(np.eye(H, dtype=np.float32), np.full((DK, DK), 1.0 / DK, np.float32))
    consts = np.zeros((P + 1, 3 * P), np.float32)
    consts[0:P] = np.concatenate([eye, eye - block, block], axis=1)
    consts[P, 0:E * E] = np.tril(np.ones((E, E), np.float32), -1).reshape(-1)
    got = dict(x=x, vecs=vecs, b1=b1, mats=mats, w1=w1, w2=w2, b2=a[F0 + "b2"], gate_w=a[F0 + "gate_w"], rows=rows, gate_b=a[F0 + "gate_b"],
               w4=w4, consts=consts)
    return {f"{n}_dram": np.ascontiguousarray(t) for n, t in got.items()}


def kernel(**inputs):
    import concourse.bacc as bacc
    from concourse.bass_utils import run_bass_kernel_spmd

    arrays = layout(inputs)
    nc = bacc.Bacc("TRN2", target_bir_lowering=False, num_devices=1)
    aps = [nc.dram_tensor(n, t.shape, mybir.dt.from_np(t.dtype), kind="ExternalInput").ap() for n, t in arrays.items()]
    out = nc.dram_tensor(_OUT, arrays["x_dram"].shape, F32, kind="ExternalOutput").ap()
    build(nc, *aps, out)
    r = run_bass_kernel_spmd(nc, [arrays], core_ids=[0])
    return r.results[0][_OUT].reshape(np.asarray(inputs["L0_attn_x"]).shape)
```
